# Optimizing a Trainium2 kernel written in Bass

```python
import numpy as np
import jax
import jax.numpy as jnp

def _softmax(x, axis=-1):
    return jax.nn.softmax(x, axis=axis)

def _gelu(x):
    return jax.nn.gelu(x, approximate=True)

def _silu(x):
    return jax.nn.silu(x)

def _sigmoid(x):
    return jax.nn.sigmoid(x)

def _layernorm(x, axis=-1, eps=1e-05):
    m = jnp.mean(x, axis=axis, keepdims=True)
    v = jnp.var(x, axis=axis, keepdims=True)
    return (x - m) / jnp.sqrt(v + eps)

def _scatter_add(tgt, idx, src, axis=0):
    return tgt.at[idx].add(src)

def _segment_sum(src, seg, n):
    return jax.ops.segment_sum(src, seg, n)
kernel_name = 'mk_cond_seq_d1_seqx_r2_f2cc4d'

def setup_inputs(seed: int=0):
    np.random.seed(seed)
    _w = jnp.asarray

    def _rec_inputs():
        import jax
        import jax.numpy as jnp
        _rk = jax.random.key(seed)
        x = -1.528e-05 + 0.9999 * jax.random.normal(jax.random.fold_in(_rk, 1), (128, 128, 1024), jnp.float32)
        _lenS = 128 - jax.random.randint(jax.random.fold_in(_rk, 7), (128,), 0, max(1, 128 // 4) + 1, jnp.int32)
        _lenS2 = 128 - jax.random.randint(jax.random.fold_in(_rk, 8), (128,), 0, max(1, 128 // 4) + 1, jnp.int32)
        itok_B_1_2 = jax.random.randint(jax.random.fold_in(_rk, 11), (128,), 1, 3, jnp.int32)
        return (x, itok_B_1_2)
    x, itok_B_1_2 = _rec_inputs()

    def _L0_cond_setup():
        import jax, jax.numpy as jnp
        import numpy as np
        H = 1024
        K = 512
        R = 3
        B = 8
        S = 1024
        LN_EPS = 1e-05
        key = jax.random.key(seed)
        ks = jax.random.split(key, 8)
        sd_d = 1.0 / np.sqrt(H)
        sd_u = 1.0 / np.sqrt(K)
        return {'role': jax.random.randint(ks[0], (B,), 0, R), 'hidden_states': jax.random.normal(ks[1], (B, S, H), dtype=jnp.float32), 'W_down': jax.random.uniform(ks[2], (R, H, K), jnp.float32, -sd_d, sd_d), 'b_down': jax.random.uniform(ks[3], (R, K), jnp.float32, -sd_d, sd_d), 'W_up': jax.random.uniform(ks[4], (R, K, H), jnp.float32, -sd_u, sd_u), 'b_up': jax.random.uniform(ks[5], (R, H), jnp.float32, -sd_u, sd_u), 'gamma': jnp.ones((R, H), jnp.float32), 'beta': jnp.zeros((R, H), jnp.float32)}
    _L0_cond_all = _L0_cond_setup()
    _L0_cond_in = {k: v for k, v in _L0_cond_all.items() if k in ('W_down', 'b_down', 'W_up', 'b_up', 'gamma', 'beta')}
    del _L0_cond_all
    return {'x': x, 'itok_B_1_2': itok_B_1_2, 'L0_cond_W_down': _L0_cond_in['W_down'], 'L0_cond_b_down': _L0_cond_in['b_down'], 'L0_cond_W_up': _L0_cond_in['W_up'], 'L0_cond_b_up': _L0_cond_in['b_up'], 'L0_cond_gamma': _L0_cond_in['gamma'], 'L0_cond_beta': _L0_cond_in['beta']}

def reference(x, itok_B_1_2, L0_cond_W_down, L0_cond_b_down, L0_cond_W_up, L0_cond_b_up, L0_cond_gamma, L0_cond_beta):
    import jax
    import jax.numpy as jnp

    def _L0_cond_ref(role, hidden_states, W_down, b_down, W_up, b_up, gamma, beta):
        import jax, jax.numpy as jnp
        import numpy as np
        H = 1024
        K = 512
        R = 3
        B = 8
        S = 1024
        LN_EPS = 1e-05
        h = jnp.einsum('bsh,bhk->bsk', hidden_states, W_down[role]) + b_down[role][:, None, :]
        h = jax.nn.gelu(h, approximate=False)
        u = jnp.einsum('bsk,bkh->bsh', h, W_up[role]) + b_up[role][:, None, :]
        y = hidden_states + u
        mean = jnp.mean(y, axis=-1, keepdims=True)
        var = jnp.mean(jnp.square(y - mean), axis=-1, keepdims=True)
        yn = (y - mean) * jax.lax.rsqrt(var + LN_EPS)
        return yn * gamma[role][:, None, :] + beta[role][:, None, :]
    x = _L0_cond_ref(itok_B_1_2, x, L0_cond_W_down, L0_cond_b_down, L0_cond_W_up, L0_cond_b_up, L0_cond_gamma, L0_cond_beta)
    return x

_drawn_inputs = setup_inputs


def setup_inputs(seed=0):
    import zlib

    import numpy as np

    out = dict(_drawn_inputs(seed))
    spreads = {'L0_cond_gamma': (1.0, 0.2), 'L0_cond_beta': (0.0, 0.1)}
    factors = {'L0_cond_b_down': 8.0}
    for name, (base, spread) in spreads.items():
        noise = np.random.default_rng([zlib.crc32(name.encode()), seed]).standard_normal(out[name].shape)
        drawn = base * np.exp(spread * noise) if base else spread * noise
        out[name] = jnp.asarray(drawn.astype(out[name].dtype))
    for name, factor in factors.items():
        out[name] = (out[name] * factor).astype(out[name].dtype)
    return out
```

```python
from contextlib import ExitStack

import concourse.bass as bass
from concourse import mybir

F32 = mybir.dt.float32
F32R = mybir.dt.float32r
I32 = mybir.dt.int32
ALU = mybir.AluOpType
ACT = mybir.ActivationFunctionType

P = 128
BLK = 32
NQ = P // BLK
LN_EPS = 1e-05
RSQRT_SEED = 0x5F3759DF - (1 << 22) - (1 << 31)


def adapter_kernel(nc, x, role, W_down, b_down, W_up, b_up, gamma, beta, out):
    B, T, H = x.shape
    R, _, K = W_down.shape
    FC, PC = H, H // 2
    assert T == P and B <= P and B % 2 == 0 and B >= 8 and R == 3
    HC = H // P
    KC = K // P
    QH = H // NQ
    NH = H // 512
    DN = HC * K // PC
    UN = KC * H // PC
    FD = HC * K // FC
    FU = KC * H // FC

    with ExitStack() as ctx:
        def sb(name, shape, dt=F32):
            return ctx.enter_context(nc.sbuf_tensor(name, shape, dt))

        def psum(name, cols):
            return ctx.enter_context(nc.psum_tensor(name, [P, cols], F32))

        def sem(name):
            return ctx.enter_context(nc.semaphore(name))

        wd_hi = sb("wd_hi", [P, 2 * HC * K], F32R)
        wd_lo = sb("wd_lo", [P, 2 * HC * K], F32R)
        wu_hi = sb("wu_hi", [P, 2 * KC * H], F32R)
        wu_lo = sb("wu_lo", [P, 2 * KC * H], F32R)
        bd_all = sb("bd_all", [P, 2 * K])
        bu_all = sb("bu_all", [P, 2 * H])
        gamma_all = sb("gamma_all", [P, 2 * H])
        beta_all = sb("beta_all", [P, 2 * H])
        x_quad = [sb(f"x_quad{i}", [P, NQ, QH]) for i in range(2)]
        xT_raw = sb("xT_raw", [P, HC, T])
        xT_hi = sb("xT_hi", [P, HC, T], F32R)
        xT_lo = sb("xT_lo", [P, HC, T], F32R)
        h = sb("h", [P, K])
        hT_hi = sb("hT_hi", [P, KC, T], F32R)
        hT_lo = sb("hT_lo", [P, KC, T], F32R)
        x_nat = [sb(f"x_nat{i}", [P, H]) for i in range(2)]
        y = [sb(f"y{i}", [P, H]) for i in range(2)]
        w_raw = [sb(f"w_raw{i}", [P, PC]) for i in range(2)]
        ident = sb("ident", [P, P])
        ysum = sb("ysum", [P, 2])
        neg_mean = sb("neg_mean", [P, 2])
        sqsum = sb("sqsum", [P, 2])
        half_var = sb("half_var", [P, 2])
        shifted = sb("shifted", [P, 2], I32)
        rstd = sb("rstd", [P, 2])
        newton = sb("newton", [P, 2])
        table = sb("table", [1, 3 * B + 1], I32)
        role_col = sb("role_col", [P, 1], I32)
        iota_col = sb("iota_col", [P, 1], I32)
        rank = sb("rank", [P, 1])
        key_col = sb("key_col", [P, 1])
        n_first_col = sb("n_first_col", [P, 1])
        opener = sb("opener", [P, 3])
        order_cols = sb("order_cols", [P, 3])
        scratch = x_quad[0][:, :, :].rearrange("p g f -> p (g f)")
        role_row, iota_row, key_row, cmp_row, onehot = (scratch[:, n * P:n * P + B] for n in range(5))
        role_row, iota_row = role_row.bitcast(I32), iota_row.bitcast(I32)

        p_down = psum("p_down", K)
        p_hT = psum("p_hT", KC * T)
        p_up = [psum(f"p_up{i}", H) for i in range(2)]
        p_sq = psum("p_sq", H)

        roles_loaded, iotas_ready, ident_zeroed = sem("roles_loaded"), sem("iotas_ready"), sem("ident_zeroed")
        sort_step, order_ready = sem("sort_step"), sem("order_ready")
        order_in_psum, table_ready = sem("order_in_psum"), sem("table_ready")
        first_raw = [sem(f"first_raw{i}") for i in range(4)]
        first_hi, first_split = sem("first_hi"), sem("first_split")
        pool_raw = [sem(f"pool_raw{i}") for i in range(2)]
        pool_hi, down_split, up_split = sem("pool_hi"), sem("down_split"), sem("up_split")
        params_loaded, slot_free = sem("params_loaded"), sem("slot_free")
        quad_loaded = [sem(f"quad_loaded{i}") for i in range(2)]
        nat_loaded = [sem(f"nat_loaded{i}") for i in range(2)]
        stored = [sem(f"stored{i}") for i in range(2)]
        x_transposed, x_hi_ready, x_lo_ready = sem("x_transposed"), sem("x_hi_ready"), sem("x_lo_ready")
        down_done, biased, gelu_done = sem("down_done"), sem("biased"), sem("gelu_done")
        h_transposed, h_hi_ready, h_lo_ready = sem("h_transposed"), sem("h_hi_ready"), sem("h_lo_ready")
        up_done, x_plus_bias, y_ready, mean_ready = sem("up_done"), sem("x_plus_bias"), sem("y_ready"), sem("mean_ready")
        squared, rstd_step, scaled, out_ready = sem("squared"), sem("rstd_step"), sem("scaled"), sem("out_ready")
        RSTD_STEPS = 9

        def seq(p, k, d):
            return 2 * p + k + d, p + (k + d) // 2, (k + d) % 2

        def live(b):
            return not isinstance(b, int) or 0 <= b < B

        def pipeline(eng, body, first, last):
            for i in range(first, 4):
                body(i // 2, i % 2)
            with eng.Fori(2, B // 2 - 1) as p:
                body(p, 0)
                body(p, 1)
            for i in range(B - 2, last + 1):
                body(i // 2, i % 2)

        def look_up(eng, row, b, most):
            at = row * B + b
            src = table[0:1, at:at + 1] if isinstance(b, int) else table[0:1, bass.ds(at, 1)]
            return eng.value_load(src, min_val=0, max_val=most)

        def cols(t, start, size):
            return t[:, start:start + size] if isinstance(start, int) else t[:, bass.ds(start, size)]

        wd_view = W_down.rearrange("r (q c a) k -> r q a c k", q=NQ, a=BLK)
        wu_view = W_up.rearrange("r (c p) h -> r c p h", p=P)
        x_view = x.rearrange("b (g t) (q f) -> b q t g f", g=NQ, q=NQ)

        block = ctx.enter_context(nc.Block())

        @block.sync
        def _(sp):
            sp.dma_start(role_row[0:B, :], role.partition_broadcast(B)).then_inc(roles_loaded, 16)
            sp.dma_start(role_col[0:B, :], role.rearrange("(b o) -> b o", o=1)).then_inc(roles_loaded, 16)

            def load_first(n):
                buf = (y + x_nat)[n % 4]
                if n >= 4:
                    sp.wait_ge(first_split, n - 3)
                if n < FD:
                    w = FC // K
                    for q in range(NQ):
                        dst = buf[BLK * q:BLK * q + BLK, 0:FC].rearrange("p (c k) -> p c k", c=w)
                        sp.dma_start(dst, wd_view[R - 1, q, :, n * w:n * w + w, :]).then_inc(first_raw[n % 4], 16)
                else:
                    m = n - FD
                    sp.dma_start(buf[:, 0:FC], wu_view[R - 1, m]).then_inc(first_raw[n % 4], 16)

            for n in range(4):
                load_first(n)
            sp.wait_ge(table_ready, 1)

            def body(p, k):
                b, half, par = seq(p, k, 2)
                if live(b):
                    if not isinstance(b, int) or b >= 2:
                        sp.wait_ge(x_transposed, b - 1)
                    n = look_up(sp, 0, b, B - 1)
                    for q in range(NQ):
                        src = x_view[bass.ds(n, 1), q].rearrange("o t g f -> (o t) g f")
                        sp.dma_start(x_quad[par][BLK * q:BLK * q + BLK, :, :], src).then_inc(quad_loaded[par], 16)
                if isinstance(p, int) and 2 * p + k == -1:
                    for n in range(4, FD + FU):
                        load_first(n)
                b, half, par = seq(p, k, 0)
                if live(b):
                    if isinstance(b, int) and b < 2:
                        sp.wait_ge(first_split, FD + FU)
                    else:
                        sp.wait_ge(y_ready, b - 1)
                    n = look_up(sp, 0, b, B - 1)
                    sp.dma_start(x_nat[par][:, :], x[bass.ds(n, 1), :, :].rearrange("o t h -> (o t) h")).then_inc(
                        nat_loaded[par], 16)
                b, half, par = seq(p, k, -2)
                if live(b):
                    n = look_up(sp, 0, b, B - 1)
                    sp.wait_ge(out_ready, b + 2)
                    sp.dma_start(out[bass.ds(n, 1), :, :].rearrange("o t h -> (o t) h"), y[par][:, :]).then_inc(
                        stored[par], 16)

            body(-1, 0)
            pipeline(sp, body, -1, B + 1)
            for par in range(2):
                sp.wait_ge(stored[par], 16 * (B // 2))

        @block.gpsimd
        def _(pool):
            pool.iota(iota_row[0:B, :], [[1, B]], base=0, channel_multiplier=0).then_inc(iotas_ready, 1)
            pool.iota(iota_col[:, :], [[0, 1]], base=0, channel_multiplier=1).then_inc(iotas_ready, 1)
            pool.memset(ident[:, :], 0.0).then_inc(ident_zeroed, 1)
            pool.memset(opener[:, 0:1], 0.0).then_inc(down_split, 1)
            pool.memset(opener[:, 1:2], 0.0).then_inc(up_split, 1)
            pool.wait_ge(ident_zeroed, 1)
            pool.affine_select(out=ident[:, :], in_=ident[:, :], compare_op=ALU.not_equal, fill=1.0, base=0,
                               pattern=[[-1, P]], channel_multiplier=1).then_inc(ident_zeroed, 1)

            def load_params(step):
                r, slot = R - 1 - step, step % 2
                for dst, src, n in ((bd_all, b_down, K), (bu_all, b_up, H), (gamma_all, gamma, H), (beta_all, beta, H)):
                    pool.dma_start(dst[:, slot * n:slot * n + n], src[r].partition_broadcast(P)).then_inc(params_loaded, 16)

            load_params(0)
            pool.wait_ge(table_ready, 1)
            n_first = pool.value_load(table[0:1, 3 * B:3 * B + 1], min_val=0, max_val=B)

            def split_piece(par, raw_count, hi_count, hi, lo, start, split):
                pool.wait_ge(pool_raw[par], raw_count)
                pool.tensor_copy(cols(hi, start, PC), w_raw[par][:, :]).then_inc(pool_hi, 1)
                pool.wait_ge(pool_hi, hi_count)
                pool.tensor_tensor(cols(lo, start, PC), w_raw[par][:, :], cols(hi, start, PC).bitcast(F32),
                                   ALU.subtract).then_inc(split, 1)

            for step in range(1, R):
                r, slot = R - 1 - step, step % 2
                pool.wait_ge(params_loaded, 64 * step)
                if step == 2:
                    pool.wait_ge(first_split, FD + FU)
                    pool.wait_ge(up_done, n_first + 1)
                    pool.wait_ge(out_ready, n_first + 1)
                    pool.tensor_tensor(opener[:, 0:1], opener[:, 0:1], opener[:, 1:2], ALU.add).then_inc(slot_free, 1)
                    pool.wait_ge(slot_free, 1)
                load_params(step)
                raw0 = (step - 1) * (DN // 2 * 64 + UN // 2 * 16)
                with pool.Fori(0, DN // 2) as m:
                    pool.wait_ge(up_split, (step - 1) * UN + 1)
                    pool.wait_ge(down_split, (step - 1) * DN + 2 * m + 1)
                    for par in range(2):
                        for q in range(NQ):
                            src = wd_view[r, q, :, bass.ds(2 * m + par, 1), :].rearrange("a c k -> a (c k)")
                            pool.dma_start(w_raw[par][BLK * q:BLK * q + BLK, :], src).then_inc(pool_raw[par], 16)
                    for par in range(2):
                        split_piece(par, raw0 + 64 * m + 64, (step - 1) * (DN + UN) + 2 * m + par + 1, wd_hi, wd_lo,
                                    slot * HC * K + 2 * PC * m + PC * par, down_split)
                with pool.Fori(0, UN // 2) as m:
                    pool.wait_ge(down_split, step * DN + 1)
                    pool.wait_ge(up_split, (step - 1) * UN + 2 * m + 1)
                    for par in range(2):
                        src = wu_view[r, bass.ds(m, 1), :, PC * par:PC * par + PC].rearrange("o p h -> (o p) h")
                        pool.dma_start(w_raw[par][:, :], src).then_inc(pool_raw[par], 16)
                    for par in range(2):
                        split_piece(par, raw0 + DN // 2 * 64 + 16 * m + 16,
                                    (step - 1) * (DN + UN) + DN + 2 * m + par + 1, wu_hi, wu_lo,
                                    slot * KC * H + 2 * PC * m + PC * par, up_split)

        def first_piece(n):
            buf = (y + x_nat)[n % 4][:, 0:FC]
            if n < FD:
                return buf, wd_hi[:, n * FC:n * FC + FC], wd_lo[:, n * FC:n * FC + FC], 16 * NQ
            m = n - FD
            return buf, wu_hi[:, m * FC:m * FC + FC], wu_lo[:, m * FC:m * FC + FC], 16 * NQ * (FD > n - 4) + 16

        @block.scalar
        def _(act):
            for n in range(FD + FU):
                buf, hi, lo, count = first_piece(n)
                act.wait_ge(first_raw[n % 4], count)
                act.activation(hi, buf, ACT.Copy).then_inc(first_hi, 1)
                if n == FD - 1:
                    act.wait_ge(x_transposed, 1)
                    act.activation(xT_hi[:, :, :], xT_raw[:, :, :], ACT.Copy).then_inc(x_hi_ready, 1)

            def body(p, k):
                b, half, par = seq(p, k, -1)
                if live(b):
                    act.wait_ge(h_transposed, b + 1)
                    act.activation(hT_hi[:, :, :].rearrange("p c t -> p (c t)"), p_hT[:, :], ACT.Copy).then_inc(h_hi_ready, 1)
                b, half, par = seq(p, k, -2)
                if live(b):
                    act.wait_ge(mean_ready, b + 1)
                    act.activation(p_sq[:, :], y[par][:, :], ACT.Square, bias=neg_mean[:, par:par + 1],
                                   accum_out=sqsum[:, par:par + 1]).then_inc(squared, 1)
                b, half, par = seq(p, k, 1)
                if live(b):
                    act.wait_ge(x_transposed, b + 1)
                    act.wait_ge(down_done, b)
                    act.activation(xT_hi[:, :, :], xT_raw[:, :, :], ACT.Copy).then_inc(x_hi_ready, 1)
                b, half, par = seq(p, k, 0)
                if live(b):
                    act.wait_ge(biased, b + 1)
                    act.activation(h[:, :], h[:, :], ACT.Gelu).then_inc(gelu_done, 1)

            pipeline(act, body, 0, B + 1)

        @block.vector
        def _(dve):
            steps = [0]

            def chain(ins):
                steps[0] += 1
                ins.then_inc(sort_step, 1)
                dve.wait_ge(sort_step, steps[0])

            dve.wait_ge(roles_loaded, 32)
            dve.wait_ge(iotas_ready, 2)
            dve.tensor_scalar(key_row[0:B, :], role_row[0:B, :], 0, R - 1, ALU.max, ALU.min)
            chain(dve.tensor_scalar(key_col[0:B, :], role_col[0:B, :], 0, R - 1, ALU.max, ALU.min))
            dve.tensor_copy(order_cols[0:B, 0:1], iota_col[0:B, :])
            chain(dve.tensor_scalar(order_cols[0:B, 1:2], key_col[0:B, :], -1.0, float(R - 1), ALU.mult, ALU.add))
            chain(dve.tensor_scalar(order_cols[0:B, 2:3], order_cols[0:B, 1:2], -1.0, 2.0, ALU.mult, ALU.add))
            chain(dve.tensor_tensor(order_cols[0:B, 2:3], order_cols[0:B, 1:2], order_cols[0:B, 2:3], ALU.mult))
            chain(dve.tensor_scalar(cmp_row[0:B, :], key_row[0:B, :], float(R - 1), None, ALU.is_equal, ALU.add,
                                    accum_out=n_first_col[0:B, :]))
            chain(dve.scalar_tensor_tensor(key_row[0:B, :], key_row[0:B, :], -float(B), iota_row[0:B, :], ALU.mult, ALU.add))
            chain(dve.scalar_tensor_tensor(key_col[0:B, :], key_col[0:B, :], -float(B), iota_col[0:B, :], ALU.mult, ALU.add))
            chain(dve.tensor_scalar(cmp_row[0:B, :], key_row[0:B, :], key_col[0:B, :], None, ALU.is_lt, ALU.add,
                                    accum_out=rank[0:B, :]))
            dve.tensor_scalar(onehot[0:B, :], iota_row[0:B, :], rank[0:B, :], None, ALU.is_equal).then_inc(order_ready, 1)
            dve.wait_ge(order_in_psum, 1)
            chain(dve.tensor_copy(table[0:1, 3 * B:3 * B + 1], n_first_col[0:1, :]))
            dve.tensor_copy(table[0:1, 0:3 * B], p_down[0:1, 0:3 * B]).then_inc(table_ready, 1)
            dve.memset(opener[:, 2:3], 0.0).then_inc(out_ready, 1)

            def split_first(n):
                buf, hi, lo, _ = first_piece(n)
                dve.wait_ge(first_hi, n + 1)
                dve.tensor_tensor(lo, buf, hi.bitcast(F32), ALU.subtract).then_inc(first_split, 1)

            def transpose_x(p, k, d):
                b, half, par = seq(p, k, d)
                dve.wait_ge(quad_loaded[par], 16 * NQ * (half + 1))
                if not isinstance(b, int) or b >= 1:
                    dve.wait_ge(x_lo_ready, b)
                dve.transpose(xT_raw[:, :, :].rearrange("p c (g t) -> p g c t", g=NQ),
                              x_quad[par][:, :, :].rearrange("p g (c a) -> p g c a", a=BLK)).then_inc(x_transposed, 1)

            def split_x(b):
                dve.wait_ge(x_hi_ready, b + 1)
                dve.tensor_tensor(xT_lo[:, :, :], xT_raw[:, :, :], xT_hi[:, :, :].bitcast(F32),
                                  ALU.subtract).then_inc(x_lo_ready, 1)

            for n in range(FD - 1):
                split_first(n)
            transpose_x(0, 0, 0)
            split_first(FD - 1)
            split_x(0)
            for n in range(FD, FD + FU):
                split_first(n)

            def body(p, k):
                b, half, par = seq(p, k, -1)
                if live(b):
                    dve.wait_ge(h_hi_ready, b + 1)
                    dve.tensor_tensor(hT_lo[:, :, :].rearrange("p c t -> p (c t)"), p_hT[:, :],
                                      hT_hi[:, :, :].rearrange("p c t -> p (c t)").bitcast(F32), ALU.subtract).then_inc(h_lo_ready, 1)

                b, half, par = seq(p, k, -2)
                if live(b):
                    dve.wait_ge(up_done, b + 2)
                    dve.wait_ge(x_plus_bias, b + 1)
                    if not isinstance(b, int) or b >= 2:
                        dve.wait_ge(stored[par], 16 * half)
                    dve.scalar_tensor_tensor(y[par][:, :], p_up[par][:, :], 1.0, x_nat[par][:, :], ALU.mult, ALU.add,
                                             accum_out=ysum[:, par:par + 1]).then_inc(y_ready, 1)
                    dve.wait_ge(y_ready, b + 1)
                    dve.tensor_scalar(neg_mean[:, par:par + 1], ysum[:, par:par + 1], -1.0 / H, None,
                                      ALU.mult).then_inc(mean_ready, 1)

                if live(seq(p, k, 1)[0]) and not (isinstance(p, int) and 2 * p + k == -1):
                    transpose_x(p, k, 1)

                if live(b):
                    slot = look_up(dve, 2, b, 1)
                    dve.wait_ge(squared, b + 1)
                    dve.scalar_tensor_tensor(y[par][:, :], y[par][:, :], neg_mean[:, par:par + 1],
                                             cols(gamma_all, slot * H, H), ALU.add, ALU.mult).then_inc(scaled, 1)
                    one = slice(par, par + 1)
                    w, r, a = half_var[:, one], rstd[:, one], newton[:, one]
                    done = RSTD_STEPS * b
                    dve.tensor_scalar(w, sqsum[:, one], 0.5 / H, 0.5 * LN_EPS, ALU.mult, ALU.add).then_inc(rstd_step, 1)
                    dve.wait_ge(rstd_step, done + 1)
                    dve.tensor_scalar(shifted[:, one], w.bitcast(I32), 1, None, ALU.logical_shift_right).then_inc(rstd_step, 1)
                    dve.wait_ge(rstd_step, done + 2)
                    dve.tensor_scalar(r.bitcast(I32), shifted[:, one], -1.0, float(RSQRT_SEED), ALU.mult,
                                      ALU.add).then_inc(rstd_step, 1)
                    for n in range(3):
                        dve.wait_ge(rstd_step, done + 3 + 2 * n)
                        dve.tensor_scalar(a, r, r, w, ALU.mult, ALU.mult).then_inc(rstd_step, 1)
                        dve.wait_ge(rstd_step, done + 4 + 2 * n)
                        dve.tensor_scalar(r, a, 1.5, r, ALU.subtract, ALU.mult).then_inc(rstd_step, 1)

                b0, _, _ = seq(p, k, 0)
                if live(b0):
                    step = look_up(dve, 1, b0, R - 1)
                    slot0 = look_up(dve, 2, b0, 1)
                    dve.wait_ge(params_loaded, 64 * step + 64)
                    dve.wait_ge(down_done, b0 + 1)
                    dve.tensor_tensor(h[:, :], p_down[:, :], cols(bd_all, slot0 * K, K), ALU.add).then_inc(biased, 1)

                if live(seq(p, k, 1)[0]):
                    split_x(seq(p, k, 1)[0])

                if live(b):
                    dve.wait_ge(scaled, b + 1)
                    dve.wait_ge(rstd_step, RSTD_STEPS * b + RSTD_STEPS)
                    dve.scalar_tensor_tensor(y[par][:, :], y[par][:, :], rstd[:, par:par + 1], cols(beta_all, slot * H, H),
                                             ALU.mult, ALU.add).then_inc(out_ready, 1)

                b, half, par = seq(p, k, -1)
                if live(b):
                    slot = look_up(dve, 2, b, 1)
                    dve.wait_ge(nat_loaded[par], 16 * (half + 1))
                    dve.tensor_tensor(x_nat[par][:, :], x_nat[par][:, :], cols(bu_all, slot * H, H), ALU.add).then_inc(x_plus_bias, 1)

            pipeline(dve, body, 0, B + 1)

        @block.tensor
        def _(pe):
            pe.wait_ge(order_ready, 1)
            for n in range(3):
                mm = pe.matmul(p_down[0:1, n * B:n * B + B], order_cols[0:B, n:n + 1], onehot[0:B, :], start=True, stop=True)
                if n == 0:
                    mm.then_inc(up_done, 1)
            mm.then_inc(order_in_psum, 1)
            pe.wait_ge(table_ready, 1)
            pe.wait_ge(ident_zeroed, 2)

            def product(dst, a_hi, a_lo, w_hi, w_lo, first, last):
                pe.matmul(dst, a_hi, w_hi, start=first, stop=False)
                pe.matmul(dst, a_hi, w_lo, start=False, stop=False)
                return pe.matmul(dst, a_lo, w_hi, start=False, stop=last)

            def body(p, k):
                b, _, _ = seq(p, k, 0)
                if live(b):
                    step, slot = look_up(pe, 1, b, R - 1), look_up(pe, 2, b, 1)
                    pe.wait_ge(down_split, DN * step + 1)
                    pe.wait_ge(x_lo_ready, b + 1)
                    for c in range(HC):
                        if isinstance(b, int) and b == 0 and c % (FC // K) == 0:
                            pe.wait_ge(first_split, c // (FC // K) + 1)
                        at = slot * HC * K + c * K
                        mm = product(p_down[:, :], xT_hi[:, c, :], xT_lo[:, c, :], cols(wd_hi, at, K), cols(wd_lo, at, K),
                                     c == 0, c == HC - 1)
                    mm.then_inc(down_done, 1)
                b, _, par = seq(p, k, -1)
                if live(b):
                    step, slot = look_up(pe, 1, b, R - 1), look_up(pe, 2, b, 1)
                    if isinstance(b, int) and b == 0:
                        pe.wait_ge(first_split, FD + FU)
                    pe.wait_ge(up_split, UN * step + 1)
                    pe.wait_ge(h_lo_ready, b + 1)
                    if not isinstance(b, int) or b >= 2:
                        pe.wait_ge(y_ready, b - 1)
                    for n in range(NH):
                        for c in range(KC):
                            at = slot * KC * H + c * H + n * 512
                            mm = product(p_up[par][:, n * 512:n * 512 + 512], hT_hi[:, c, :], hT_lo[:, c, :],
                                         cols(wu_hi, at, 512), cols(wu_lo, at, 512), c == 0, c == KC - 1)
                    mm.then_inc(up_done, 1)
                b, _, _ = seq(p, k, 0)
                if live(b):
                    pe.wait_ge(gelu_done, b + 1)
                    for c in range(KC):
                        mm = pe.transpose(p_hT[:, c * T:c * T + T], h[:, c * P:c * P + P], ident[:, :])
                    mm.then_inc(h_transposed, 1)

            pipeline(pe, body, 0, B)


_INS = ["x", "itok_B_1_2", "L0_cond_W_down", "L0_cond_b_down", "L0_cond_W_up", "L0_cond_b_up", "L0_cond_gamma", "L0_cond_beta"]


def kernel(**inputs):
    import numpy as _np
    import concourse.bacc as _bacc
    from concourse import mybir as _mybir
    from concourse.bass_utils import run_bass_kernel_spmd as _run

    nc = _bacc.Bacc("TRN2", target_bir_lowering=False, num_devices=1)
    arrays, args = {}, []
    for name in _INS:
        a = _np.ascontiguousarray(inputs[name])
        arrays[f"in_{name}"] = a
        args.append(nc.dram_tensor(f"in_{name}", a.shape, _mybir.dt.from_np(a.dtype), kind="ExternalInput").ap())
    out = nc.dram_tensor("out", inputs["x"].shape, _mybir.dt.float32, kind="ExternalOutput").ap()
    adapter_kernel(nc, *args, out)
    return _run(nc, [arrays], core_ids=[0]).results[0]["out"]
```

```python
from contextlib import ExitStack

import concourse.bass as bass
from concourse import mybir

F32 = mybir.dt.float32
F32R = mybir.dt.float32r
I32 = mybir.dt.int32
ALU = mybir.AluOpType
ACT = mybir.ActivationFunctionType

P = 128
BLK = 32
NQ = P // BLK
LN_EPS = 1e-05
NEWTON = 3
RSQRT_SEED = 0x5F3759DF - (1 << 22) - (1 << 30)


def adapter_kernel(nc, x, role, W_down, b_down, W_up, b_up, gamma, beta, out):
    B, T, H = x.shape
    R, _, K = W_down.shape
    FC, PC = H, H // 2
    assert T == P and B <= P and B % 2 == 0 and B >= 8 and R == 3
    HC = H // P
    KC = K // P
    QH = H // NQ
    NH = H // 512
    DN = HC * K // PC
    UN = KC * H // PC
    FD = HC * K // FC
    FU = KC * H // FC

    with ExitStack() as ctx:
        def sb(name, shape, dt=F32):
            return ctx.enter_context(nc.sbuf_tensor(name, shape, dt))

        def psum(name, cols):
            return ctx.enter_context(nc.psum_tensor(name, [P, cols], F32))

        def sem(name):
            return ctx.enter_context(nc.semaphore(name))

        wd_hi = sb("wd_hi", [P, 2 * HC * K], F32R)
        wd_lo = sb("wd_lo", [P, 2 * HC * K], F32R)
        wu_hi = sb("wu_hi", [P, 2 * KC * H], F32R)
        wu_lo = sb("wu_lo", [P, 2 * KC * H], F32R)
        BD, BU, GAMMA, BETA, PARAMS = 0, K, K + H, K + 2 * H, K + 3 * H
        params = sb("params", [P, 2 * PARAMS])
        x_quad = [sb(f"x_quad{i}", [P, NQ, QH]) for i in range(2)]
        xT_raw = sb("xT_raw", [P, HC, T])
        xT_hi = sb("xT_hi", [P, HC, T], F32R)
        xT_lo = sb("xT_lo", [P, HC, T], F32R)
        h = sb("h", [P, K])
        hT_hi = sb("hT_hi", [P, KC, T], F32R)
        hT_lo = sb("hT_lo", [P, KC, T], F32R)
        x_nat = [sb(f"x_nat{i}", [P, H]) for i in range(2)]
        y = [sb(f"y{i}", [P, H]) for i in range(2)]
        w_raw = [sb(f"w_raw{i}", [P, PC]) for i in range(2)]
        ident = sb("ident", [P, P])
        ysum = sb("ysum", [P, 2])
        neg_mean = sb("neg_mean", [P, 2])
        sqsum = sb("sqsum", [P, 2])
        neg_half_var = sb("neg_half_var", [P, 2])
        rstd = [sb(f"rstd{n}", [P, 2]) for n in range(NEWTON + 1)]
        rstd_sq = sb("rstd_sq", [P, 2])
        factor = sb("factor", [P, 2])
        NUMBER, WEIGHTS_AT, PARAMS_AT, WHEN_SPLIT, WHEN_LOADED, ROWS = range(6)
        table = sb("table", [1, ROWS * B + 1], I32)
        role_col = sb("role_col", [P, 1], I32)
        iota_col = sb("iota_col", [P, 1], I32)
        rank = sb("rank", [P, 1])
        key_col = sb("key_col", [P, 1])
        n_first_col = sb("n_first_col", [P, 1])
        opener = sb("opener", [P, 3])
        step_col = sb("step_col", [P, 1])
        slot_col = sb("slot_col", [P, 1])
        order_cols = sb("order_cols", [P, ROWS])
        scratch = x_quad[0][:, :, :].rearrange("p g f -> p (g f)")
        role_row, iota_row, key_row, cmp_row, onehot = (scratch[:, n * P:n * P + B] for n in range(5))
        role_row, iota_row = role_row.bitcast(I32), iota_row.bitcast(I32)

        p_down = psum("p_down", K)
        p_hT = psum("p_hT", KC * T)
        p_up = [psum(f"p_up{i}", H) for i in range(2)]
        p_sq = psum("p_sq", H)

        roles_loaded, iotas_ready, ident_zeroed = sem("roles_loaded"), sem("iotas_ready"), sem("ident_zeroed")
        sort_step, order_ready = sem("sort_step"), sem("order_ready")
        order_in_psum, table_ready = sem("order_in_psum"), sem("table_ready")
        first_raw = [sem(f"first_raw{i}") for i in range(4)]
        first_hi, first_split = sem("first_hi"), sem("first_split")
        pool_raw = [sem(f"pool_raw{i}") for i in range(2)]
        pool_hi, pieces_split = sem("pool_hi"), sem("pieces_split")
        params_loaded, slot_free = sem("params_loaded"), sem("slot_free")
        quad_loaded = [sem(f"quad_loaded{i}") for i in range(2)]
        nat_loaded = [sem(f"nat_loaded{i}") for i in range(2)]
        stored = [sem(f"stored{i}") for i in range(2)]
        x_transposed, x_hi_ready, x_lo_ready = sem("x_transposed"), sem("x_hi_ready"), sem("x_lo_ready")
        down_done, biased, gelu_done = sem("down_done"), sem("biased"), sem("gelu_done")
        h_transposed, h_hi_ready, h_lo_ready = sem("h_transposed"), sem("h_hi_ready"), sem("h_lo_ready")
        up_done, x_plus_bias, y_ready, mean_ready = sem("up_done"), sem("x_plus_bias"), sem("y_ready"), sem("mean_ready")
        squared, scaled, out_ready = sem("squared"), sem("scaled"), sem("out_ready")
        half_var_ready = sem("half_var_ready")
        rstd_ready = [sem(f"rstd_ready{n}") for n in range(NEWTON + 1)]
        square_ready = [sem(f"square_ready{n}") for n in range(NEWTON)]
        factor_ready = [sem(f"factor_ready{n}") for n in range(NEWTON)]

        def seq(i, k, d):
            return i + k + d, 8 * i + 16 * ((k + d) // 2), (k + d) % 2

        def live(b):
            return not isinstance(b, int) or 0 <= b < B

        def late(b, least):
            return not isinstance(b, int) or b >= least

        def pipeline(eng, body, first, last):
            for i in range(first, 4):
                body(i - i % 2, i % 2)
            with eng.Fori(4, B - 2, 2) as i:
                body(i, 0)
                body(i, 1)
            for i in range(B - 2, last + 1):
                body(i - i % 2, i % 2)

        def look_up(eng, row, b, least, most):
            at = row * B + b
            src = table[0:1, at:at + 1] if isinstance(b, int) else table[0:1, bass.ds(at, 1)]
            return eng.value_load(src, min_val=least, max_val=most)

        def cols(t, start, size):
            return t[:, start:start + size] if isinstance(start, int) else t[:, bass.ds(start, size)]

        wd_view = W_down.rearrange("r (q c a) k -> r q a c k", q=NQ, a=BLK)
        wu_view = W_up.rearrange("r (c p) h -> r c p h", p=P)
        x_view = x.rearrange("b (g t) (q f) -> b q t g f", g=NQ, q=NQ)

        block = ctx.enter_context(nc.Block())

        @block.sync
        def _(sp):
            sp.dma_start(role_row[0:B, :], role.partition_broadcast(B)).then_inc(roles_loaded, 16)
            sp.dma_start(role_col[0:B, :], role.rearrange("(b o) -> b o", o=1)).then_inc(roles_loaded, 16)

            def load_first(n):
                buf = (y + x_nat)[n % 4]
                if n >= 4:
                    sp.wait_ge(first_split, n - 3)
                if n < FD:
                    w = FC // K
                    for q in range(NQ):
                        dst = buf[BLK * q:BLK * q + BLK, 0:FC].rearrange("p (c k) -> p c k", c=w)
                        sp.dma_start(dst, wd_view[R - 1, q, :, n * w:n * w + w, :]).then_inc(first_raw[n % 4], 16)
                else:
                    m = n - FD
                    sp.dma_start(buf[:, 0:FC], wu_view[R - 1, m]).then_inc(first_raw[n % 4], 16)

            for n in range(4):
                load_first(n)
            sp.wait_ge(table_ready, 1)

            def body(i, k):
                b, _, par = seq(i, k, 2)
                if live(b):
                    n = look_up(sp, NUMBER, b, 0, B - 1)
                    if late(b, 2):
                        sp.wait_ge(x_transposed, b - 1)
                    for q in range(NQ):
                        src = x_view[bass.ds(n, 1), q].rearrange("o t g f -> (o t) g f")
                        sp.dma_start(x_quad[par][BLK * q:BLK * q + BLK, :, :], src).then_inc(quad_loaded[par], 16)
                if isinstance(i, int) and i + k == -1:
                    for n in range(4, FD + FU):
                        load_first(n)
                b, _, par = seq(i, k, -3)
                if live(b):
                    n = look_up(sp, NUMBER, b, 0, B - 1)
                    sp.wait_ge(out_ready, b + 2)
                    sp.dma_start(out[bass.ds(n, 1), :, :].rearrange("o t h -> (o t) h"), y[par][:, :]).then_inc(
                        stored[par], 16)
                b, _, par = seq(i, k, 0)
                if live(b):
                    n = look_up(sp, NUMBER, b, 0, B - 1)
                    if late(b, 2):
                        sp.wait_ge(y_ready, b - 1)
                    else:
                        sp.wait_ge(first_split, FD + FU)
                    sp.dma_start(x_nat[par][:, :], x[bass.ds(n, 1), :, :].rearrange("o t h -> (o t) h")).then_inc(
                        nat_loaded[par], 16)

            body(-2, 0)
            pipeline(sp, body, -1, B + 2)
            for par in range(2):
                sp.wait_ge(stored[par], 16 * (B // 2))

        @block.gpsimd
        def _(pool):
            pool.iota(iota_row[0:B, :], [[1, B]], base=0, channel_multiplier=0).then_inc(iotas_ready, 1)
            pool.iota(iota_col[:, :], [[0, 1]], base=0, channel_multiplier=1).then_inc(iotas_ready, 1)
            pool.memset(ident[:, :], 0.0).then_inc(ident_zeroed, 1)
            pool.memset(opener[:, 0:2], 0.0).then_inc(pieces_split, 1)
            pool.wait_ge(ident_zeroed, 1)
            pool.affine_select(out=ident[:, :], in_=ident[:, :], compare_op=ALU.not_equal, fill=1.0, base=0,
                               pattern=[[-1, P]], channel_multiplier=1).then_inc(ident_zeroed, 1)

            def load_params(step):
                r, slot = R - 1 - step, step % 2
                for at, src, n in ((BD, b_down, K), (BU, b_up, H), (GAMMA, gamma, H), (BETA, beta, H)):
                    at += slot * PARAMS
                    pool.dma_start(params[:, at:at + n], src[r].partition_broadcast(P)).then_inc(params_loaded, 16)

            load_params(0)
            pool.wait_ge(table_ready, 1)
            n_first = pool.value_load(table[0:1, ROWS * B:ROWS * B + 1], min_val=0, max_val=B)

            def split_piece(par, raw_count, count, hi, lo, start):
                pool.wait_ge(pool_raw[par], raw_count)
                pool.tensor_copy(cols(hi, start, PC), w_raw[par][:, :]).then_inc(pool_hi, 1)
                pool.wait_ge(pool_hi, count)
                pool.tensor_tensor(cols(lo, start, PC), w_raw[par][:, :], cols(hi, start, PC).bitcast(F32),
                                   ALU.subtract).then_inc(pieces_split, 1)

            for step in range(1, R):
                r, slot = R - 1 - step, step % 2
                pool.wait_ge(params_loaded, 64 * step)
                if step == 2:
                    pool.wait_ge(first_split, FD + FU)
                    pool.wait_ge(up_done, n_first + 1)
                    pool.wait_ge(out_ready, n_first + 1)
                    pool.tensor_tensor(opener[:, 0:1], opener[:, 0:1], opener[:, 1:2], ALU.add).then_inc(slot_free, 1)
                    pool.wait_ge(slot_free, 1)
                load_params(step)
                raw0 = (step - 1) * (DN // 2 * 64 + UN // 2 * 16)
                done = (step - 1) * (DN + UN)
                with pool.Fori(0, DN // 2) as m:
                    for par in range(2):
                        for q in range(NQ):
                            src = wd_view[r, q, :, bass.ds(2 * m + par, 1), :].rearrange("a c k -> a (c k)")
                            pool.dma_start(w_raw[par][BLK * q:BLK * q + BLK, :], src).then_inc(pool_raw[par], 16)
                    for par in range(2):
                        split_piece(par, raw0 + 64 * m + 64, done + 2 * m + par + 1, wd_hi, wd_lo,
                                    slot * HC * K + 2 * PC * m + PC * par)
                    pool.wait_ge(pieces_split, done + 2 * m + 3)
                raw0 += DN // 2 * 64
                done += DN
                with pool.Fori(0, UN // 2) as m:
                    for par in range(2):
                        src = wu_view[r, bass.ds(m, 1), :, PC * par:PC * par + PC].rearrange("o p h -> (o p) h")
                        pool.dma_start(w_raw[par][:, :], src).then_inc(pool_raw[par], 16)
                    for par in range(2):
                        split_piece(par, raw0 + 16 * m + 16, done + 2 * m + par + 1, wu_hi, wu_lo,
                                    slot * KC * H + 2 * PC * m + PC * par)
                    pool.wait_ge(pieces_split, done + 2 * m + 3)

        def first_piece(n):
            buf = (y + x_nat)[n % 4][:, 0:FC]
            if n < FD:
                return buf, wd_hi[:, n * FC:n * FC + FC], wd_lo[:, n * FC:n * FC + FC], 16 * NQ
            m = n - FD
            return buf, wu_hi[:, m * FC:m * FC + FC], wu_lo[:, m * FC:m * FC + FC], 16 * NQ * (FD > n - 4) + 16

        @block.scalar
        def _(act):
            for n in range(FD + FU):
                buf, hi, lo, count = first_piece(n)
                act.wait_ge(first_raw[n % 4], count)
                act.activation(hi, buf, ACT.Copy).then_inc(first_hi, 1)
                if n == FD - 1:
                    act.wait_ge(x_transposed, 1)
                    act.activation(xT_hi[:, :, :], xT_raw[:, :, :], ACT.Copy).then_inc(x_hi_ready, 1)

            def body(i, k):
                b, _, par = seq(i, k, -1)
                if live(b):
                    act.wait_ge(h_transposed, b + 1)
                    act.activation(hT_hi[:, :, :].rearrange("p c t -> p (c t)"), p_hT[:, :], ACT.Copy).then_inc(h_hi_ready, 1)
                b, _, par = seq(i, k, -2)
                if live(b):
                    act.wait_ge(mean_ready, b + 1)
                    act.activation(p_sq[:, :], y[par][:, :], ACT.Square, bias=neg_mean[:, par:par + 1],
                                   accum_out=sqsum[:, par:par + 1]).then_inc(squared, 1)
                b, _, par = seq(i, k, 1)
                if live(b):
                    act.wait_ge(x_transposed, b + 1)
                    act.wait_ge(down_done, b)
                    act.activation(xT_hi[:, :, :], xT_raw[:, :, :], ACT.Copy).then_inc(x_hi_ready, 1)
                b, _, par = seq(i, k, 0)
                if live(b):
                    act.wait_ge(biased, b + 1)
                    act.activation(h[:, :], h[:, :], ACT.Gelu).then_inc(gelu_done, 1)
                b, _, par = seq(i, k, -2)
                if live(b):
                    one = slice(par, par + 1)
                    v = neg_half_var[:, one]
                    act.wait_ge(squared, b + 1)
                    act.activation(v, sqsum[:, one], ACT.Copy, scale=-0.5 / H, bias=-0.5 * LN_EPS).then_inc(half_var_ready, 1)
                    act.wait_ge(half_var_ready, b + 1)
                    act.activation(rstd[0][:, one].bitcast(I32), v.bitcast(I32), ACT.Copy, scale=-0.5,
                                   bias=float(RSQRT_SEED)).then_inc(rstd_ready[0], 1)
                    for n in range(NEWTON):
                        r = rstd[n][:, one]
                        act.wait_ge(rstd_ready[n], b + 1)
                        act.activation(rstd_sq[:, one], r, ACT.Square).then_inc(square_ready[n], 1)
                        act.wait_ge(square_ready[n], b + 1)
                        act.activation(factor[:, one], rstd_sq[:, one], ACT.Copy, scale=v, bias=1.5).then_inc(factor_ready[n], 1)
                        act.wait_ge(factor_ready[n], b + 1)
                        act.activation(rstd[n + 1][:, one], r, ACT.Copy, scale=factor[:, one]).then_inc(rstd_ready[n + 1], 1)

            pipeline(act, body, 0, B + 1)

        @block.vector
        def _(dve):
            steps = [0]

            def chain(ins):
                steps[0] += 1
                ins.then_inc(sort_step, 1)
                dve.wait_ge(sort_step, steps[0])

            dve.wait_ge(roles_loaded, 32)
            dve.wait_ge(iotas_ready, 2)
            dve.tensor_scalar(key_row[0:B, :], role_row[0:B, :], 0, R - 1, ALU.max, ALU.min)
            chain(dve.tensor_scalar(key_col[0:B, :], role_col[0:B, :], 0, R - 1, ALU.max, ALU.min))
            dve.tensor_copy(order_cols[0:B, NUMBER:NUMBER + 1], iota_col[0:B, :])
            chain(dve.tensor_scalar(step_col[0:B, :], key_col[0:B, :], -1.0, float(R - 1), ALU.mult, ALU.add))
            chain(dve.tensor_scalar(slot_col[0:B, :], step_col[0:B, :], -1.0, 2.0, ALU.mult, ALU.add))
            chain(dve.tensor_tensor(slot_col[0:B, :], step_col[0:B, :], slot_col[0:B, :], ALU.mult))
            for row, col, scale, offset in ((WEIGHTS_AT, slot_col, HC * K, 0), (PARAMS_AT, slot_col, PARAMS, 0),
                                            (WHEN_SPLIT, step_col, DN + UN, 1), (WHEN_LOADED, step_col, 64, 64)):
                dve.tensor_scalar(order_cols[0:B, row:row + 1], col[0:B, :], float(scale), float(offset), ALU.mult, ALU.add)
            chain(dve.tensor_scalar(cmp_row[0:B, :], key_row[0:B, :], float(R - 1), None, ALU.is_equal, ALU.add,
                                    accum_out=n_first_col[0:B, :]))
            chain(dve.scalar_tensor_tensor(key_row[0:B, :], key_row[0:B, :], -float(B), iota_row[0:B, :], ALU.mult, ALU.add))
            chain(dve.scalar_tensor_tensor(key_col[0:B, :], key_col[0:B, :], -float(B), iota_col[0:B, :], ALU.mult, ALU.add))
            chain(dve.tensor_scalar(cmp_row[0:B, :], key_row[0:B, :], key_col[0:B, :], None, ALU.is_lt, ALU.add,
                                    accum_out=rank[0:B, :]))
            dve.tensor_scalar(onehot[0:B, :], iota_row[0:B, :], rank[0:B, :], None, ALU.is_equal).then_inc(order_ready, 1)
            dve.wait_ge(order_in_psum, 1)
            chain(dve.tensor_copy(table[0:1, ROWS * B:ROWS * B + 1], n_first_col[0:1, :]))
            dve.tensor_copy(table[0:1, 0:ROWS * B], p_up[0][0:1, 0:ROWS * B]).then_inc(table_ready, 1)
            dve.memset(opener[:, 2:3], 0.0).then_inc(out_ready, 1)

            def split_first(n):
                buf, hi, lo, _ = first_piece(n)
                dve.wait_ge(first_hi, n + 1)
                dve.tensor_tensor(lo, buf, hi.bitcast(F32), ALU.subtract).then_inc(first_split, 1)

            def transpose_x(i, k):
                b, half16, par = seq(i, k, 0)
                dve.wait_ge(quad_loaded[par], NQ * half16 + 16 * NQ)
                if late(b, 1):
                    dve.wait_ge(x_lo_ready, b)
                dve.transpose(xT_raw[:, :, :].rearrange("p c (g t) -> p g c t", g=NQ),
                              x_quad[par][:, :, :].rearrange("p g (c a) -> p g c a", a=BLK)).then_inc(x_transposed, 1)

            def split_x(b):
                dve.wait_ge(x_hi_ready, b + 1)
                dve.tensor_tensor(xT_lo[:, :, :], xT_raw[:, :, :], xT_hi[:, :, :].bitcast(F32),
                                  ALU.subtract).then_inc(x_lo_ready, 1)

            for n in range(FD - 1):
                split_first(n)
            transpose_x(0, 0)
            split_first(FD - 1)
            split_x(0)
            for n in range(FD, FD + FU):
                split_first(n)

            def body(i, k):
                at = {}
                for d in (-3, -2, -1, 0):
                    b = seq(i, k, d)[0]
                    if live(b):
                        at[d] = look_up(dve, PARAMS_AT, b, 0, PARAMS)
                b = seq(i, k, 0)[0]
                if live(b):
                    when_loaded = look_up(dve, WHEN_LOADED, b, 64, 64 * R)

                b, _, par = seq(i, k, -1)
                if live(b):
                    dve.wait_ge(h_hi_ready, b + 1)
                    dve.tensor_tensor(hT_lo[:, :, :].rearrange("p c t -> p (c t)"), p_hT[:, :],
                                      hT_hi[:, :, :].rearrange("p c t -> p (c t)").bitcast(F32), ALU.subtract).then_inc(h_lo_ready, 1)

                b, _, par = seq(i, k, -3)
                if live(b):
                    dve.wait_ge(scaled, b + 1)
                    dve.wait_ge(rstd_ready[NEWTON], b + 1)
                    dve.scalar_tensor_tensor(y[par][:, :], y[par][:, :], rstd[NEWTON][:, par:par + 1],
                                             cols(params, at[-3] + BETA, H), ALU.mult, ALU.add).then_inc(out_ready, 1)

                b, half16, par = seq(i, k, -2)
                if live(b):
                    dve.wait_ge(up_done, b + 2)
                    dve.wait_ge(x_plus_bias, b + 1)
                    if late(b, 2):
                        dve.wait_ge(stored[par], half16)
                    dve.scalar_tensor_tensor(y[par][:, :], p_up[par][:, :], 1.0, x_nat[par][:, :], ALU.mult, ALU.add,
                                             accum_out=ysum[:, par:par + 1]).then_inc(y_ready, 1)
                    dve.wait_ge(y_ready, b + 1)
                    dve.tensor_scalar(neg_mean[:, par:par + 1], ysum[:, par:par + 1], -1.0 / H, None,
                                      ALU.mult).then_inc(mean_ready, 1)

                if live(seq(i, k, 1)[0]):
                    transpose_x(i, k + 1)

                b, half16, par = seq(i, k, -1)
                if live(b):
                    dve.wait_ge(nat_loaded[par], half16 + 16)
                    dve.tensor_tensor(x_nat[par][:, :], x_nat[par][:, :], cols(params, at[-1] + BU, H),
                                      ALU.add).then_inc(x_plus_bias, 1)

                b, _, _ = seq(i, k, 0)
                if live(b):
                    dve.wait_ge(params_loaded, when_loaded)
                    dve.wait_ge(down_done, b + 1)
                    dve.tensor_tensor(h[:, :], p_down[:, :], cols(params, at[0] + BD, K), ALU.add).then_inc(biased, 1)

                if live(seq(i, k, 1)[0]):
                    split_x(seq(i, k, 1)[0])

                b, _, par = seq(i, k, -2)
                if live(b):
                    dve.wait_ge(squared, b + 1)
                    dve.scalar_tensor_tensor(y[par][:, :], y[par][:, :], neg_mean[:, par:par + 1],
                                             cols(params, at[-2] + GAMMA, H), ALU.add, ALU.mult).then_inc(scaled, 1)

            pipeline(dve, body, 0, B + 2)

        @block.tensor
        def _(pe):
            pe.wait_ge(order_ready, 1)
            for n in range(ROWS):
                mm = pe.matmul(p_up[0][0:1, n * B:n * B + B], order_cols[0:B, n:n + 1], onehot[0:B, :], start=True, stop=True)
                if n == 0:
                    mm.then_inc(up_done, 1)
            mm.then_inc(order_in_psum, 1)
            pe.wait_ge(table_ready, 1)
            pe.wait_ge(ident_zeroed, 2)

            def product(dst, a_hi, a_lo, w_hi, w_lo, first, last):
                pe.matmul(dst, a_hi, w_hi, start=first, stop=False)
                pe.matmul(dst, a_hi, w_lo, start=False, stop=False)
                return pe.matmul(dst, a_lo, w_hi, start=False, stop=last)

            def body(i, k):
                at = {}
                for d in (-1, 0):
                    b = seq(i, k, d)[0]
                    if live(b):
                        at[d] = look_up(pe, WEIGHTS_AT, b, 0, HC * K)
                b = seq(i, k, 0)[0]
                if live(b):
                    when_split = look_up(pe, WHEN_SPLIT, b, 1, (R - 1) * (DN + UN) + 1)

                b, _, _ = seq(i, k, -1)
                if live(b):
                    pe.wait_ge(gelu_done, b + 1)
                    for c in range(KC):
                        mm = pe.transpose(p_hT[:, c * T:c * T + T], h[:, c * P:c * P + P], ident[:, :])
                    mm.then_inc(h_transposed, 1)

                b, _, _ = seq(i, k, 0)
                if live(b):
                    pe.wait_ge(pieces_split, when_split)
                    pe.wait_ge(x_lo_ready, b + 1)
                    for c in range(HC):
                        if isinstance(b, int) and b == 0 and c % (FC // K) == 0:
                            pe.wait_ge(first_split, c // (FC // K) + 1)
                        mm = product(p_down[:, :], xT_hi[:, c, :], xT_lo[:, c, :], cols(wd_hi, at[0] + c * K, K),
                                     cols(wd_lo, at[0] + c * K, K), c == 0, c == HC - 1)
                    mm.then_inc(down_done, 1)

                b, _, par = seq(i, k, -1)
                if live(b):
                    if isinstance(b, int) and b == 0:
                        pe.wait_ge(first_split, FD + FU)
                    pe.wait_ge(h_lo_ready, b + 1)
                    if late(b, 2):
                        pe.wait_ge(y_ready, b - 1)
                    for n in range(NH):
                        for c in range(KC):
                            off = at[-1] + c * H + n * 512
                            mm = product(p_up[par][:, n * 512:n * 512 + 512], hT_hi[:, c, :], hT_lo[:, c, :],
                                         cols(wu_hi, off, 512), cols(wu_lo, off, 512), c == 0, c == KC - 1)
                    mm.then_inc(up_done, 1)

            pipeline(pe, body, 0, B)


_INS = ["x", "itok_B_1_2", "L0_cond_W_down", "L0_cond_b_down", "L0_cond_W_up", "L0_cond_b_up", "L0_cond_gamma", "L0_cond_beta"]


def kernel(**inputs):
    import numpy as _np
    import concourse.bacc as _bacc
    from concourse import mybir as _mybir
    from concourse.bass_utils import run_bass_kernel_spmd as _run

    nc = _bacc.Bacc("TRN2", target_bir_lowering=False, num_devices=1)
    arrays, args = {}, []
    for name in _INS:
        a = _np.ascontiguousarray(inputs[name])
        arrays[f"in_{name}"] = a
        args.append(nc.dram_tensor(f"in_{name}", a.shape, _mybir.dt.from_np(a.dtype), kind="ExternalInput").ap())
    out = nc.dram_tensor("out", inputs["x"].shape, _mybir.dt.float32, kind="ExternalOutput").ap()
    adapter_kernel(nc, *args, out)
    return _run(nc, [arrays], core_ids=[0]).results[0]["out"]
```

```python
from contextlib import ExitStack

import concourse.bass as bass
from concourse import mybir

F32 = mybir.dt.float32
F32R = mybir.dt.float32r
I32 = mybir.dt.int32
ALU = mybir.AluOpType
ACT = mybir.ActivationFunctionType

P = 128
BLK = 32
NQ = P // BLK
LN_EPS = 1e-05
NEWTON = 3
RSQRT_SEED = 0x5F3759DF - (1 << 22) - (1 << 30)


def adapter_kernel(nc, x, role, W_down, b_down, W_up, b_up, gamma, beta, out):
    B, T, H = x.shape
    R, _, K = W_down.shape
    FC, PC = H, H // 2
    assert T == P and B <= P and B % 2 == 0 and B >= 8 and R == 3
    HC = H // P
    KC = K // P
    QH = H // NQ
    NH = H // 512
    DN = HC * K // PC
    UN = KC * H // PC
    FD = HC * K // FC
    FU = KC * H // FC
    EARLY = FD // 2
    LATE = FD + FU // 2

    with ExitStack() as ctx:
        def sb(name, shape, dt=F32):
            return ctx.enter_context(nc.sbuf_tensor(name, shape, dt))

        def psum(name, cols):
            return ctx.enter_context(nc.psum_tensor(name, [P, cols], F32))

        def sem(name):
            return ctx.enter_context(nc.semaphore(name))

        wd_hi = sb("wd_hi", [P, 2 * HC * K], F32R)
        wd_lo = sb("wd_lo", [P, 2 * HC * K], F32R)
        wu_hi = sb("wu_hi", [P, 2 * KC * H], F32R)
        wu_lo = sb("wu_lo", [P, 2 * KC * H], F32R)
        BD, BU, GAMMA, BETA, PARAMS = 0, K, K + H, K + 2 * H, K + 3 * H
        params = sb("params", [P, 2 * PARAMS])
        x_quad = [sb(f"x_quad{i}", [P, NQ, QH]) for i in range(2)]
        xT_raw = sb("xT_raw", [P, HC, T])
        xT_hi = sb("xT_hi", [P, HC, T], F32R)
        xT_lo = sb("xT_lo", [P, HC, T], F32R)
        h = sb("h", [P, K])
        hT_hi = sb("hT_hi", [P, KC, T], F32R)
        hT_lo = sb("hT_lo", [P, KC, T], F32R)
        x_nat = [sb(f"x_nat{i}", [P, H]) for i in range(2)]
        y = [sb(f"y{i}", [P, H]) for i in range(2)]
        w_raw = [sb(f"w_raw{i}", [P, PC]) for i in range(2)]
        ident = sb("ident", [P, P])
        ysum = sb("ysum", [P, 2])
        neg_mean = sb("neg_mean", [P, 2])
        sqsum = sb("sqsum", [P, 2])
        neg_half_var = sb("neg_half_var", [P, 2])
        rstd = [sb(f"rstd{n}", [P, 2]) for n in range(NEWTON + 1)]
        rstd_sq = sb("rstd_sq", [P, 2])
        factor = sb("factor", [P, 2])
        NUMBER, WEIGHTS_AT, PARAMS_AT, WHEN_SPLIT, WHEN_LOADED, ROWS = range(6)
        table = sb("table", [1, ROWS * B + 1], I32)
        role_col = sb("role_col", [P, 1], I32)
        iota_col = sb("iota_col", [P, 1], I32)
        rank = sb("rank", [P, 1])
        key_col = sb("key_col", [P, 1])
        n_first_col = sb("n_first_col", [P, 1])
        opener = sb("opener", [P, 3])
        step_col = sb("step_col", [P, 1])
        slot_col = sb("slot_col", [P, 1])
        order_cols = sb("order_cols", [P, ROWS])
        scratch = x_quad[1][:, :, :].rearrange("p g f -> p (g f)")
        role_row, iota_row, key_row, cmp_row, onehot = (scratch[:, n * P:n * P + B] for n in range(5))
        role_row, iota_row = role_row.bitcast(I32), iota_row.bitcast(I32)

        p_down = psum("p_down", K)
        p_hT = psum("p_hT", KC * T)
        p_up = [psum(f"p_up{i}", H) for i in range(2)]
        p_sq = psum("p_sq", H)

        roles_loaded, iotas_ready, ident_zeroed = sem("roles_loaded"), sem("iotas_ready"), sem("ident_zeroed")
        sort_step, order_ready = sem("sort_step"), sem("order_ready")
        order_in_psum, table_ready = sem("order_in_psum"), sem("table_ready")
        first_raw = [sem(f"first_raw{i}") for i in range(4)]
        first_hi, first_split = sem("first_hi"), sem("first_split")
        pool_raw = [sem(f"pool_raw{i}") for i in range(2)]
        pool_hi, pieces_split = sem("pool_hi"), sem("pieces_split")
        bias_loaded, params_loaded, slot_free = sem("bias_loaded"), sem("params_loaded"), sem("slot_free")
        quad_loaded = [sem(f"quad_loaded{i}") for i in range(2)]
        nat_loaded = [sem(f"nat_loaded{i}") for i in range(2)]
        stored = [sem(f"stored{i}") for i in range(2)]
        x_transposed, x_hi_ready, x_lo_ready = sem("x_transposed"), sem("x_hi_ready"), sem("x_lo_ready")
        down_done, biased, gelu_done = sem("down_done"), sem("biased"), sem("gelu_done")
        h_transposed, h_hi_ready, h_lo_ready = sem("h_transposed"), sem("h_hi_ready"), sem("h_lo_ready")
        up_done, x_plus_bias, y_ready, mean_ready = sem("up_done"), sem("x_plus_bias"), sem("y_ready"), sem("mean_ready")
        squared, scaled, out_ready = sem("squared"), sem("scaled"), sem("out_ready")
        half_var_ready = sem("half_var_ready")
        rstd_ready = [sem(f"rstd_ready{n}") for n in range(NEWTON + 1)]
        square_ready = [sem(f"square_ready{n}") for n in range(NEWTON)]
        factor_ready = [sem(f"factor_ready{n}") for n in range(NEWTON)]

        def seq(i, k, d):
            return i + k + d, 8 * i + 16 * ((k + d) // 2), (k + d) % 2

        def live(b):
            return not isinstance(b, int) or 0 <= b < B

        def late(b, least):
            return not isinstance(b, int) or b >= least

        def pipeline(eng, body, first, last):
            for i in range(first, 4):
                body(i - i % 2, i % 2)
            with eng.Fori(4, B - 2, 2) as i:
                body(i, 0)
                body(i, 1)
            for i in range(B - 2, last + 1):
                body(i - i % 2, i % 2)

        def look_up(eng, row, b, least, most):
            at = row * B + b
            src = table[0:1, at:at + 1] if isinstance(b, int) else table[0:1, bass.ds(at, 1)]
            return eng.value_load(src, min_val=least, max_val=most)

        def cols(t, start, size):
            return t[:, start:start + size] if isinstance(start, int) else t[:, bass.ds(start, size)]

        wd_view = W_down.rearrange("r (q c a) k -> r q a c k", q=NQ, a=BLK)
        wu_view = W_up.rearrange("r (c p) h -> r c p h", p=P)
        x_view = x.rearrange("b (g t) (q f) -> b q t g f", g=NQ, q=NQ)

        block = ctx.enter_context(nc.Block())

        @block.sync
        def _(sp):
            sp.dma_start(role_row[0:B, :], role.partition_broadcast(B)).then_inc(roles_loaded, 16)
            sp.dma_start(role_col[0:B, :], role.rearrange("(b o) -> b o", o=1)).then_inc(roles_loaded, 16)

            def load_first(n):
                buf = (y + x_nat)[n % 4]
                if n >= 4:
                    sp.wait_ge(first_split, n - 3)
                if n < FD:
                    w = FC // K
                    for q in range(NQ):
                        dst = buf[BLK * q:BLK * q + BLK, 0:FC].rearrange("p (c k) -> p c k", c=w)
                        sp.dma_start(dst, wd_view[R - 1, q, :, n * w:n * w + w, :]).then_inc(first_raw[n % 4], 16)
                else:
                    m = n - FD
                    sp.dma_start(buf[:, 0:FC], wu_view[R - 1, m]).then_inc(first_raw[n % 4], 16)

            for n in range(EARLY):
                load_first(n)
            sp.wait_ge(table_ready, 1)

            def body(i, k):
                b, _, par = seq(i, k, 2)
                if live(b):
                    n = look_up(sp, NUMBER, b, 0, B - 1)
                    if late(b, 2):
                        sp.wait_ge(x_transposed, b - 1)
                    elif b == 1:
                        sp.wait_ge(table_ready, 2)
                    for q in range(NQ):
                        src = x_view[bass.ds(n, 1), q].rearrange("o t g f -> (o t) g f")
                        sp.dma_start(x_quad[par][BLK * q:BLK * q + BLK, :, :], src).then_inc(quad_loaded[par], 16)
                if isinstance(i, int) and i + k < 0:
                    for n in (range(EARLY, LATE), range(LATE, FD + FU))[i + k + 2]:
                        load_first(n)
                b, _, par = seq(i, k, -3)
                if live(b):
                    n = look_up(sp, NUMBER, b, 0, B - 1)
                    sp.wait_ge(out_ready, b + 2)
                    sp.dma_start(out[bass.ds(n, 1), :, :].rearrange("o t h -> (o t) h"), y[par][:, :]).then_inc(
                        stored[par], 16)
                b, _, par = seq(i, k, 0)
                if live(b):
                    n = look_up(sp, NUMBER, b, 0, B - 1)
                    if late(b, 2):
                        sp.wait_ge(y_ready, b - 1)
                    else:
                        sp.wait_ge(first_split, FD + FU)
                    sp.dma_start(x_nat[par][:, :], x[bass.ds(n, 1), :, :].rearrange("o t h -> (o t) h")).then_inc(
                        nat_loaded[par], 16)

            body(-2, 0)
            pipeline(sp, body, -1, B + 2)
            for par in range(2):
                sp.wait_ge(stored[par], 16 * (B // 2))

        @block.gpsimd
        def _(pool):
            pool.iota(iota_row[0:B, :], [[1, B]], base=0, channel_multiplier=0).then_inc(iotas_ready, 1)
            pool.iota(iota_col[:, :], [[0, 1]], base=0, channel_multiplier=1).then_inc(iotas_ready, 1)
            pool.memset(ident[:, :], 0.0).then_inc(ident_zeroed, 1)
            pool.memset(opener[:, 0:2], 0.0).then_inc(pieces_split, 1)
            pool.wait_ge(ident_zeroed, 1)
            pool.affine_select(out=ident[:, :], in_=ident[:, :], compare_op=ALU.not_equal, fill=1.0, base=0,
                               pattern=[[-1, P]], channel_multiplier=1).then_inc(ident_zeroed, 1)

            def load_bias(step):
                at = step % 2 * PARAMS + BD
                pool.dma_start(params[:, at:at + K], b_down[R - 1 - step].partition_broadcast(P)).then_inc(bias_loaded, 16)

            def load_params(step):
                for at, src in ((BU, b_up), (GAMMA, gamma), (BETA, beta)):
                    at += step % 2 * PARAMS
                    pool.dma_start(params[:, at:at + H], src[R - 1 - step].partition_broadcast(P)).then_inc(params_loaded, 16)

            load_bias(0)
            pool.wait_ge(first_split, FD)
            load_params(0)
            pool.wait_ge(first_split, FD + FU)
            pool.wait_ge(table_ready, 2)
            n_first = pool.value_load(table[0:1, ROWS * B:ROWS * B + 1], min_val=0, max_val=B)

            def split_piece(par, raw_count, count, hi, lo, start):
                pool.wait_ge(pool_raw[par], raw_count)
                pool.tensor_copy(cols(hi, start, PC), w_raw[par][:, :]).then_inc(pool_hi, 1)
                pool.wait_ge(pool_hi, count)
                pool.tensor_tensor(cols(lo, start, PC), w_raw[par][:, :], cols(hi, start, PC).bitcast(F32),
                                   ALU.subtract).then_inc(pieces_split, 1)

            for step in range(1, R):
                r, slot = R - 1 - step, step % 2
                pool.wait_ge(bias_loaded, 16 * step)
                pool.wait_ge(params_loaded, 48 * step)
                if step == 2:
                    pool.wait_ge(first_split, FD + FU)
                    pool.wait_ge(up_done, n_first + 1)
                    pool.wait_ge(out_ready, n_first + 1)
                    pool.tensor_tensor(opener[:, 0:1], opener[:, 0:1], opener[:, 1:2], ALU.add).then_inc(slot_free, 1)
                    pool.wait_ge(slot_free, 1)
                load_bias(step)
                load_params(step)
                raw0 = (step - 1) * (DN // 2 * 64 + UN // 2 * 16)
                done = (step - 1) * (DN + UN)
                with pool.Fori(0, DN // 2) as m:
                    for par in range(2):
                        for q in range(NQ):
                            src = wd_view[r, q, :, bass.ds(2 * m + par, 1), :].rearrange("a c k -> a (c k)")
                            pool.dma_start(w_raw[par][BLK * q:BLK * q + BLK, :], src).then_inc(pool_raw[par], 16)
                    for par in range(2):
                        split_piece(par, raw0 + 64 * m + 64, done + 2 * m + par + 1, wd_hi, wd_lo,
                                    slot * HC * K + 2 * PC * m + PC * par)
                    pool.wait_ge(pieces_split, done + 2 * m + 3)
                raw0 += DN // 2 * 64
                done += DN
                with pool.Fori(0, UN // 2) as m:
                    for par in range(2):
                        src = wu_view[r, bass.ds(m, 1), :, PC * par:PC * par + PC].rearrange("o p h -> (o p) h")
                        pool.dma_start(w_raw[par][:, :], src).then_inc(pool_raw[par], 16)
                    for par in range(2):
                        split_piece(par, raw0 + 16 * m + 16, done + 2 * m + par + 1, wu_hi, wu_lo,
                                    slot * KC * H + 2 * PC * m + PC * par)
                    pool.wait_ge(pieces_split, done + 2 * m + 3)

        def first_piece(n):
            buf = (y + x_nat)[n % 4][:, 0:FC]
            if n < FD:
                return buf, wd_hi[:, n * FC:n * FC + FC], wd_lo[:, n * FC:n * FC + FC], 16 * NQ
            m = n - FD
            return buf, wu_hi[:, m * FC:m * FC + FC], wu_lo[:, m * FC:m * FC + FC], 16 * NQ * (FD > n - 4) + 16

        @block.scalar
        def _(act):
            act.wait_ge(pieces_split, 1)
            act.activation(factor[:, 0:1], opener[:, 0:1], ACT.Gelu)

            def round_first(n):
                buf, hi, lo, count = first_piece(n)
                act.wait_ge(first_raw[n % 4], count)
                act.activation(hi, buf, ACT.Copy).then_inc(first_hi, 1)

            for n in range(EARLY):
                round_first(n)
            act.wait_ge(x_transposed, 1)
            act.activation(xT_hi[:, :, :], xT_raw[:, :, :], ACT.Copy).then_inc(x_hi_ready, 1)
            for n in range(EARLY, LATE):
                round_first(n)

            def body(i, k):
                b, _, par = seq(i, k, -1)
                if live(b):
                    act.wait_ge(h_transposed, b + 1)
                    act.activation(hT_hi[:, :, :].rearrange("p c t -> p (c t)"), p_hT[:, :], ACT.Copy).then_inc(h_hi_ready, 1)
                b, _, par = seq(i, k, -2)
                if live(b):
                    act.wait_ge(mean_ready, b + 1)
                    act.activation(p_sq[:, :], y[par][:, :], ACT.Square, bias=neg_mean[:, par:par + 1],
                                   accum_out=sqsum[:, par:par + 1]).then_inc(squared, 1)
                b, _, par = seq(i, k, 1)
                if live(b):
                    act.wait_ge(x_transposed, b + 1)
                    act.wait_ge(down_done, b)
                    act.activation(xT_hi[:, :, :], xT_raw[:, :, :], ACT.Copy).then_inc(x_hi_ready, 1)
                b, _, par = seq(i, k, 0)
                if live(b):
                    act.wait_ge(biased, b + 1)
                    act.activation(h[:, :], h[:, :], ACT.Gelu).then_inc(gelu_done, 1)
                if isinstance(i, int) and i + k == 0:
                    for n in range(LATE, FD + FU):
                        round_first(n)
                b, _, par = seq(i, k, -2)
                if live(b):
                    one = slice(par, par + 1)
                    v = neg_half_var[:, one]
                    act.wait_ge(squared, b + 1)
                    act.activation(v, sqsum[:, one], ACT.Identity, scale=-0.5 / H, bias=-0.5 * LN_EPS).then_inc(half_var_ready, 1)
                    act.wait_ge(half_var_ready, b + 1)
                    act.activation(rstd[0][:, one].bitcast(I32), v.bitcast(I32), ACT.Identity, scale=-0.5,
                                   bias=float(RSQRT_SEED)).then_inc(rstd_ready[0], 1)
                    for n in range(NEWTON):
                        r = rstd[n][:, one]
                        act.wait_ge(rstd_ready[n], b + 1)
                        act.activation(rstd_sq[:, one], r, ACT.Square).then_inc(square_ready[n], 1)
                        act.wait_ge(square_ready[n], b + 1)
                        act.activation(factor[:, one], rstd_sq[:, one], ACT.Identity, scale=v, bias=1.5).then_inc(factor_ready[n], 1)
                        act.wait_ge(factor_ready[n], b + 1)
                        act.activation(rstd[n + 1][:, one], r, ACT.Identity, scale=factor[:, one]).then_inc(rstd_ready[n + 1], 1)

            pipeline(act, body, 0, B + 1)

        @block.vector
        def _(dve):
            steps = [0]

            def chain(*group):
                for ins in group:
                    ins.then_inc(sort_step, 1)
                steps[0] += len(group)
                dve.wait_ge(sort_step, steps[0])

            dve.wait_ge(roles_loaded, 32)
            dve.wait_ge(iotas_ready, 2)
            chain(dve.tensor_scalar(key_row[0:B, :], role_row[0:B, :], 0, R - 1, ALU.max, ALU.min),
                  dve.tensor_scalar(key_col[0:B, :], role_col[0:B, :], 0, R - 1, ALU.max, ALU.min))
            chain(dve.tensor_scalar(cmp_row[0:B, :], key_row[0:B, :], float(R - 1), None, ALU.is_equal, ALU.add,
                                    accum_out=n_first_col[0:B, :]),
                  dve.tensor_scalar(step_col[0:B, :], key_col[0:B, :], -1.0, float(R - 1), ALU.mult, ALU.add))
            chain(dve.scalar_tensor_tensor(key_row[0:B, :], key_row[0:B, :], -float(B), iota_row[0:B, :], ALU.mult, ALU.add),
                  dve.scalar_tensor_tensor(key_col[0:B, :], key_col[0:B, :], -float(B), iota_col[0:B, :], ALU.mult, ALU.add),
                  dve.tensor_scalar(slot_col[0:B, :], step_col[0:B, :], -1.0, 2.0, ALU.mult, ALU.add))
            chain(dve.tensor_scalar(cmp_row[0:B, :], key_row[0:B, :], key_col[0:B, :], None, ALU.is_lt, ALU.add,
                                    accum_out=rank[0:B, :]),
                  dve.tensor_tensor(slot_col[0:B, :], step_col[0:B, :], slot_col[0:B, :], ALU.mult))
            dve.tensor_copy(order_cols[0:B, NUMBER:NUMBER + 1], iota_col[0:B, :])
            for row, col, scale, offset in ((WEIGHTS_AT, slot_col, HC * K, 0), (PARAMS_AT, slot_col, PARAMS, 0),
                                            (WHEN_SPLIT, step_col, DN + UN, 1), (WHEN_LOADED, step_col, 16, 16)):
                dve.tensor_scalar(order_cols[0:B, row:row + 1], col[0:B, :], float(scale), float(offset), ALU.mult, ALU.add)
            dve.tensor_scalar(onehot[0:B, :], iota_row[0:B, :], rank[0:B, :], None, ALU.is_equal).then_inc(order_ready, 1)
            chain(dve.tensor_copy(table[0:1, ROWS * B:ROWS * B + 1], n_first_col[0:1, :]))
            dve.wait_ge(order_in_psum, 1)
            dve.tensor_copy(table[0:1, 0:B], p_up[1][0:1, 0:B]).then_inc(table_ready, 1)
            dve.wait_ge(order_in_psum, 2)
            dve.tensor_copy(table[0:1, B:ROWS * B], p_up[0][0:1, 0:(ROWS - 1) * B]).then_inc(table_ready, 1)
            dve.memset(opener[:, 2:3], 0.0).then_inc(out_ready, 1)

            def split_first(n):
                buf, hi, lo, _ = first_piece(n)
                dve.wait_ge(first_hi, n + 1)
                dve.tensor_tensor(lo, buf, hi.bitcast(F32), ALU.subtract).then_inc(first_split, 1)

            def transpose_x(i, k):
                b, half16, par = seq(i, k, 0)
                dve.wait_ge(quad_loaded[par], NQ * half16 + 16 * NQ)
                if late(b, 1):
                    dve.wait_ge(x_lo_ready, b)
                dve.transpose(xT_raw[:, :, :].rearrange("p c (g t) -> p g c t", g=NQ),
                              x_quad[par][:, :, :].rearrange("p g (c a) -> p g c a", a=BLK)).then_inc(x_transposed, 1)

            def split_x(b):
                dve.wait_ge(x_hi_ready, b + 1)
                dve.tensor_tensor(xT_lo[:, :, :], xT_raw[:, :, :], xT_hi[:, :, :].bitcast(F32),
                                  ALU.subtract).then_inc(x_lo_ready, 1)

            for n in range(EARLY):
                split_first(n)
            transpose_x(0, 0)
            split_x(0)
            for n in range(EARLY, LATE):
                split_first(n)

            def normalise(i, k, params_at):
                b, _, par = seq(i, k, -3)
                if live(b):
                    dve.wait_ge(scaled, b + 1)
                    dve.wait_ge(rstd_ready[NEWTON], b + 1)
                    dve.scalar_tensor_tensor(y[par][:, :], y[par][:, :], rstd[NEWTON][:, par:par + 1],
                                             cols(params, params_at + BETA, H), ALU.mult, ALU.add).then_inc(out_ready, 1)

            def body(i, k):
                at = {}
                for d in (-3, -2, -1, 0):
                    b = seq(i, k, d)[0]
                    if live(b):
                        at[d] = look_up(dve, PARAMS_AT, b, 0, PARAMS)
                b = seq(i, k, 0)[0]
                if live(b):
                    when_loaded = look_up(dve, WHEN_LOADED, b, 16, 16 * R)

                b, _, par = seq(i, k, -1)
                if live(b):
                    dve.wait_ge(h_hi_ready, b + 1)
                    dve.tensor_tensor(hT_lo[:, :, :].rearrange("p c t -> p (c t)"), p_hT[:, :],
                                      hT_hi[:, :, :].rearrange("p c t -> p (c t)").bitcast(F32), ALU.subtract).then_inc(h_lo_ready, 1)

                last = isinstance(i, int) and i + k == B + 1
                if not last:
                    normalise(i, k, at.get(-3))

                b, half16, par = seq(i, k, -2)
                if live(b):
                    dve.wait_ge(up_done, b + 2)
                    dve.wait_ge(x_plus_bias, b + 1)
                    if late(b, 2):
                        dve.wait_ge(stored[par], half16)
                    dve.scalar_tensor_tensor(y[par][:, :], p_up[par][:, :], 1.0, x_nat[par][:, :], ALU.mult, ALU.add,
                                             accum_out=ysum[:, par:par + 1]).then_inc(y_ready, 1)
                    dve.wait_ge(y_ready, b + 1)
                    dve.tensor_scalar(neg_mean[:, par:par + 1], ysum[:, par:par + 1], -1.0 / H, None,
                                      ALU.mult).then_inc(mean_ready, 1)

                if last:
                    normalise(i, k, at.get(-3))

                if live(seq(i, k, 1)[0]):
                    transpose_x(i, k + 1)

                b, half16, par = seq(i, k, -1)
                if live(b):
                    if not late(b, 1):
                        dve.wait_ge(params_loaded, 3 * look_up(dve, WHEN_LOADED, b, 16, 16 * R))
                    dve.wait_ge(nat_loaded[par], half16 + 16)
                    dve.tensor_tensor(x_nat[par][:, :], x_nat[par][:, :], cols(params, at[-1] + BU, H),
                                      ALU.add).then_inc(x_plus_bias, 1)

                b, _, _ = seq(i, k, 0)
                if live(b):
                    dve.wait_ge(bias_loaded, when_loaded)
                    if late(b, 1):
                        dve.wait_ge(params_loaded, 3 * when_loaded)
                    dve.wait_ge(down_done, b + 1)
                    dve.tensor_tensor(h[:, :], p_down[:, :], cols(params, at[0] + BD, K), ALU.add).then_inc(biased, 1)

                if live(seq(i, k, 1)[0]):
                    split_x(seq(i, k, 1)[0])
                if isinstance(i, int) and i + k == 0:
                    for n in range(LATE, FD + FU):
                        split_first(n)

                b, _, par = seq(i, k, -2)
                if live(b):
                    dve.wait_ge(squared, b + 1)
                    dve.scalar_tensor_tensor(y[par][:, :], y[par][:, :], neg_mean[:, par:par + 1],
                                             cols(params, at[-2] + GAMMA, H), ALU.add, ALU.mult).then_inc(scaled, 1)

            pipeline(dve, body, 0, B + 2)

        @block.tensor
        def _(pe):
            pe.wait_ge(order_ready, 1)
            pe.matmul(p_up[1][0:1, 0:B], order_cols[0:B, NUMBER:NUMBER + 1], onehot[0:B, :], start=True,
                      stop=True).then_inc(order_in_psum, 1)
            for n in range(ROWS - 1):
                mm = pe.matmul(p_up[0][0:1, n * B:n * B + B], order_cols[0:B, n + 1:n + 2], onehot[0:B, :], start=True, stop=True)
                if n == 0:
                    mm.then_inc(up_done, 1)
            mm.then_inc(order_in_psum, 1)
            pe.wait_ge(table_ready, 2)
            pe.wait_ge(ident_zeroed, 2)

            def product(dst, a_hi, a_lo, w_hi, w_lo, first, last):
                pe.matmul(dst, a_hi, w_hi, start=first, stop=False)
                pe.matmul(dst, a_hi, w_lo, start=False, stop=False)
                return pe.matmul(dst, a_lo, w_hi, start=False, stop=last)

            def body(i, k):
                at = {}
                for d in (-1, 0):
                    b = seq(i, k, d)[0]
                    if live(b):
                        at[d] = look_up(pe, WEIGHTS_AT, b, 0, HC * K)
                b = seq(i, k, 0)[0]
                if live(b):
                    when_split = look_up(pe, WHEN_SPLIT, b, 1, (R - 1) * (DN + UN) + 1)

                b, _, _ = seq(i, k, -1)
                if live(b):
                    pe.wait_ge(gelu_done, b + 1)
                    for c in range(KC):
                        mm = pe.transpose(p_hT[:, c * T:c * T + T], h[:, c * P:c * P + P], ident[:, :])
                    mm.then_inc(h_transposed, 1)

                b, _, _ = seq(i, k, 0)
                if live(b):
                    pe.wait_ge(pieces_split, when_split)
                    pe.wait_ge(x_lo_ready, b + 1)
                    for c in range(HC):
                        if isinstance(b, int) and b == 0 and c % (FC // K) == 0:
                            pe.wait_ge(first_split, c // (FC // K) + 1)
                        mm = product(p_down[:, :], xT_hi[:, c, :], xT_lo[:, c, :], cols(wd_hi, at[0] + c * K, K),
                                     cols(wd_lo, at[0] + c * K, K), c == 0, c == HC - 1)
                    mm.then_inc(down_done, 1)

                b, _, par = seq(i, k, -1)
                if live(b):
                    if isinstance(b, int) and b == 0:
                        pe.wait_ge(first_split, FD + FU)
                    pe.wait_ge(h_lo_ready, b + 1)
                    if late(b, 2):
                        pe.wait_ge(y_ready, b - 1)
                    for n in range(NH):
                        for c in range(KC):
                            off = at[-1] + c * H + n * 512
                            mm = product(p_up[par][:, n * 512:n * 512 + 512], hT_hi[:, c, :], hT_lo[:, c, :],
                                         cols(wu_hi, off, 512), cols(wu_lo, off, 512), c == 0, c == KC - 1)
                    mm.then_inc(up_done, 1)

            pipeline(pe, body, 0, B)


_INS = ["x", "itok_B_1_2", "L0_cond_W_down", "L0_cond_b_down", "L0_cond_W_up", "L0_cond_b_up", "L0_cond_gamma", "L0_cond_beta"]


def kernel(**inputs):
    import numpy as _np
    import concourse.bacc as _bacc
    from concourse import mybir as _mybir
    from concourse.bass_utils import run_bass_kernel_spmd as _run

    nc = _bacc.Bacc("TRN2", target_bir_lowering=False, num_devices=1)
    arrays, args = {}, []
    for name in _INS:
        a = _np.ascontiguousarray(inputs[name])
        arrays[f"in_{name}"] = a
        args.append(nc.dram_tensor(f"in_{name}", a.shape, _mybir.dt.from_np(a.dtype), kind="ExternalInput").ap())
    out = nc.dram_tensor("out", inputs["x"].shape, _mybir.dt.float32, kind="ExternalOutput").ap()
    adapter_kernel(nc, *args, out)
    return _run(nc, [arrays], core_ids=[0]).results[0]["out"]
```
